# Optimizing a Trainium2 kernel written in Bass

```python
import numpy as np
import jax
import jax.numpy as jnp

def _softmax(x, axis=-1):
    return jax.nn.softmax(x, axis=axis)
def _gelu(x):
    return jax.nn.gelu(x, approximate=True)
def _silu(x):
    return jax.nn.silu(x)
def _sigmoid(x):
    return jax.nn.sigmoid(x)
def _layernorm(x, axis=-1, eps=1e-5):
    m = jnp.mean(x, axis=axis, keepdims=True)
    v = jnp.var(x, axis=axis, keepdims=True)
    return (x - m) / jnp.sqrt(v + eps)
def _scatter_add(tgt, idx, src, axis=0):
    return tgt.at[idx].add(src)
def _segment_sum(src, seg, n):
    return jax.ops.segment_sum(src, seg, n)

kernel_name = 'mk_conv_preact_d1_conv_nchw256_9e6bbb'

def setup_inputs(seed: int = 0):
    np.random.seed(seed)
    _w = jnp.asarray
    def _rec_inputs():
        import jax
        import jax.numpy as jnp
        _gk = jax.random.key(seed)
        x = -7.109e-05 + 0.9999 * jax.random.normal(jax.random.fold_in(_gk, 1), (64, 256, 64, 64), jnp.float32)
        return x
    x = _rec_inputs()
    def _L0_conv_setup():
        import jax, jax.numpy as jnp
        import numpy as np
        C = 256
        HID = 256
        key = jax.random.key(seed)
        ks = jax.random.split(key, 7)
        s1 = 1.0 / np.sqrt(2 * C)
        s2 = 1.0 / np.sqrt(HID)
        return {'features': jax.random.normal(ks[0], (64, C, 64, 64), dtype=jnp.float32), 'w1': jax.random.uniform(ks[1], (2 * C, HID), jnp.float32, -s1, s1), 'b1': jax.random.uniform(ks[2], (HID,), jnp.float32, -s1, s1), 'w2': jax.random.uniform(ks[3], (HID, HID), jnp.float32, -s2, s2), 'b2': jax.random.uniform(ks[4], (HID,), jnp.float32, -s2, s2), 'w3': jax.random.uniform(ks[5], (HID, C), jnp.float32, -s2, s2), 'b3': jax.random.uniform(ks[6], (C,), jnp.float32, -s2, s2)}
    _L0_conv_all = _L0_conv_setup()
    _L0_conv_in = {k: v for k, v in _L0_conv_all.items() if k in ('w1', 'b1', 'w2', 'b2', 'w3', 'b3', )}
    del _L0_conv_all

    return {
        "x": x,
        "L0_conv_w1": _L0_conv_in["w1"],
        "L0_conv_b1": _L0_conv_in["b1"],
        "L0_conv_w2": _L0_conv_in["w2"],
        "L0_conv_b2": _L0_conv_in["b2"],
        "L0_conv_w3": _L0_conv_in["w3"],
        "L0_conv_b3": _L0_conv_in["b3"],
    }

def reference(x, L0_conv_w1, L0_conv_b1, L0_conv_w2, L0_conv_b2, L0_conv_w3, L0_conv_b3):
    import jax
    import jax.numpy as jnp
    def _L0_conv_ref(features, w1, b1, w2, b2, w3, b3):
        import jax, jax.numpy as jnp
        import numpy as np
        C = 256
        HID = 256
        B, Cc, H, W = features.shape
        if H > 8 or W > 8:
            fs = features.reshape(B, Cc, 8, H // 8, 8, W // 8).mean(axis=(3, 5))
        else:
            fs = features
        hs, ws = (fs.shape[2], fs.shape[3])
        N = hs * ws
        pad = jnp.pad(fs, ((0, 0), (0, 0), (1, 1), (1, 1)))
        nb = jnp.stack([pad[:, :, ki:ki + hs, kj:kj + ws] for ki in range(3) for kj in range(3)], axis=2)
        nb = nb.reshape(B, Cc, 9, N).transpose(0, 3, 2, 1)
        center = fs.reshape(B, Cc, N).transpose(0, 2, 1)
        pairs = jnp.concatenate([jnp.broadcast_to(center[:, :, None, :], (B, N, 9, Cc)), nb], axis=-1)
        h = jax.nn.relu(jnp.einsum('bnkf,fh->bnkh', pairs, w1) + b1)
        h = jax.nn.relu(jnp.einsum('bnkh,hg->bnkg', h, w2) + b2)
        rel = jnp.einsum('bnkg,gc->bnkc', h, w3) + b3
        agg = rel.mean(axis=2)
        agg = agg.transpose(0, 2, 1).reshape(B, Cc, hs, ws)
        if H != hs or W != ws:
            agg = jax.image.resize(agg, (B, Cc, H, W), method='bilinear')
        return agg

    def _gn(v, G=32, eps=1e-5):
        B_, C_, H_, W_ = v.shape
        g = v.reshape(B_, G, C_ // G, H_, W_)
        m = jnp.mean(g, axis=(2, 3, 4), keepdims=True)
        s = jnp.var(g, axis=(2, 3, 4), keepdims=True)
        return ((g - m) / jnp.sqrt(s + eps)).reshape(v.shape)

    def _ln_c(v, eps=1e-6):
        m = jnp.mean(v, axis=1, keepdims=True)
        s = jnp.var(v, axis=1, keepdims=True)
        return (v - m) / jnp.sqrt(s + eps)

    def _ln_t(v, eps=1e-5):
        m = jnp.mean(v, axis=-1, keepdims=True)
        s = jnp.var(v, axis=-1, keepdims=True)
        return (v - m) / jnp.sqrt(s + eps)

    def _to_tokens(v):
        B_, C_, H_, W_ = v.shape
        return v.reshape(B_, C_, H_ * W_).transpose(0, 2, 1)
    def _from_tokens(t, like):
        B_, C_, H_, W_ = like.shape
        return t.transpose(0, 2, 1).reshape(B_, C_, H_, W_)

    x = x + _L0_conv_ref(_gn(x), L0_conv_w1, L0_conv_b1, L0_conv_w2, L0_conv_b2, L0_conv_w3, L0_conv_b3)
    return x


_drawn_inputs = setup_inputs


def setup_inputs(seed=0):
    import zlib

    import numpy as np

    out = dict(_drawn_inputs(seed))
    spreads = {}
    factors = {'L0_conv_w1': 8.0,
     'L0_conv_b1': 8.0,
     'L0_conv_w2': 7.308,
     'L0_conv_b2': 5.069,
     'L0_conv_w3': 3.109,
     'L0_conv_b3': 3.237}
    for name, (base, spread) in spreads.items():
        noise = np.random.default_rng([zlib.crc32(name.encode()), seed]).standard_normal(out[name].shape)
        drawn = base * np.exp(spread * noise) if base else spread * noise
        out[name] = jnp.asarray(drawn.astype(out[name].dtype))
    for name, factor in factors.items():
        out[name] = (out[name] * factor).astype(out[name].dtype)
    return out
```

```python
from contextlib import ExitStack

import concourse.bass as bass
from concourse import mybir


F32 = mybir.dt.float32
BF16 = mybir.dt.bfloat16
ALU = mybir.AluOpType
ACT = mybir.ActivationFunctionType
AX = mybir.AxisListType

P = 128
RING = 5
GROUPS = 32
EPS = 1e-5
GRID = 8
NB = 9
PARTS = 3
REACH = 5
CHUNK = 1024


def conv_preact_program(nc, x, w1, w2, w3, biases, up_w, group_w, part_w, out):
    B, C, H, W = x.shape
    HID = w2.shape[0]
    CT = C // P
    HT = HID // P
    PIX = H * W
    CELL = H // GRID
    POS = GRID * GRID
    AREA = CELL * CELL
    PAIRS = NB * POS
    HALVES = 2
    KPOS = REACH * GRID
    KUP = PARTS * KPOS
    NCH = PIX // CHUNK
    QN = PAIRS // 2
    SQ = PIX // 2
    PADG = GRID + 2
    assert CT == 2 and HT == 2 and B > RING and (B - 4) % RING == 0 and NCH == 4

    x_v = x.rearrange("b (t p) h w -> b t p (h w)", p=P)
    out_v = out.rearrange("b (t p) h w -> b t p (h w)", p=P)

    with ExitStack() as ctx:
        def sb(name, shape, dt=F32):
            return ctx.enter_context(nc.sbuf_tensor(name, shape, dt))

        def pb(name, shape, dt=F32):
            return ctx.enter_context(nc.psum_tensor(name, shape, dt))

        def sem(name):
            return ctx.enter_context(nc.semaphore(name))

        img = sb("img", [P, RING, CT, PIX])
        w1_sb = sb("w1_sb", [P, 2 * CT, HID])
        w2_sb = sb("w2_sb", [P, HT, HID])
        w3_sb = sb("w3_sb", [P, HT, C])
        bias_sb = sb("bias_sb", [P, HT + HT + CT])
        b1_sb, b2_sb, b3_sb = bias_sb[:, 0:HT], bias_sb[:, HT:2 * HT], bias_sb[:, 2 * HT:]
        up_sb = sb("up_sb", [KUP, PIX], BF16)
        group_sb = sb("group_sb", [P, 2, P])
        part_sb = sb("part_sb", [KUP, 2])
        half_pow = sb("half_pow", [P, CT])
        eps64 = sb("eps64", [P, CT])
        junk = sb("junk", [P, SQ], BF16)
        block_sum = sb("block_sum", [P, RING, CT, POS])
        chan_sum = sb("chan_sum", [P, RING, CT])
        shift64 = sb("shift64", [P, RING, CT])
        sq_sum = sb("sq_sum", [P, RING, CT, 2])
        moments = sb("moments", [P, 2, CT])
        st = sb("st", [P, 6, CT])
        norm = sb("norm", [P, CT, POS])
        centre = sb("centre", [P, HT, POS])
        neigh = sb("neigh", [P, HT, PADG * PADG])
        h1 = sb("h1", [P, HT, PAIRS])
        h2 = sb("h2", [P, HT, PAIRS])
        fold4 = h1[:, :, 0:4 * POS]
        fold2 = h1[:, :, 4 * POS:6 * POS]
        fold1 = h1[:, :, 6 * POS:7 * POS]
        nb_sum = sb("nb_sum", [P, HT, HALVES, PARTS, KPOS])
        agg = sb("agg", [KUP, HALVES * C])
        high = sb("high", [KUP, HALVES * C], BF16)
        rest = sb("rest", [KUP, HALVES * C])
        mid = sb("mid", [KUP, HALVES * C], BF16)
        stack = sb("stack", [KUP, RING, HALVES * C], BF16)

        up_ps = pb("up_ps", [P, 2, CHUNK])
        l2_ps = pb("l2_ps", [P, 2, 512])
        small_ps = pb("small_ps", [P, 512])
        agg_ps = pb("agg_ps", [P, HALVES * C])
        MOM, SHF, AB = 0, 8, 128

        weights_in = sem("weights_in")
        consts_set = sem("consts_set")
        load_done = [[sem(f"load_done_{s}_{t}") for t in range(CT)] for s in range(RING)]
        store_done = [[sem(f"store_done_{s}_{t}") for t in range(CT)] for s in range(RING)]
        pooled = sem("pooled")
        summed = sem("summed")
        added = sem("added")
        shift_made = sem("shift_made")
        moments_made = sem("moments_made")
        ab_made = sem("ab_made")
        shift_read = sem("shift_read")
        moments_read = sem("moments_read")
        first_read = sem("first_read")
        squared = sem("squared")
        stat_steps = sem("stat_steps")
        pairs_made = sem("pairs_made")
        h1_ready = sem("h1_ready")
        l2_made = sem("l2_made")
        h2_ready = sem("h2_ready")
        fold_steps = sem("fold_steps")
        agg_made = sem("agg_made")
        agg_read = sem("agg_read")
        rest_made = sem("rest_made")
        mid_made = sem("mid_made")
        stack_made = sem("stack_made")
        up_made = sem("up_made")

        STATS, FOLDS = 8, 4
        CH = CT * NCH

        def num(c):
            return c[0] * RING + c[1] if c[0] is not None else c[1]

        def shifted(c, d):
            return (c[0], c[1] + d)

        def slot(c):
            return c[1] % RING

        def landed(c):
            passes = c[1] // RING + 1
            return 16 * (c[0] + passes) if c[0] is not None else 16 * passes

        def steps(eng, step, tail=2):
            for k in range(2):
                step((None, k), k, None)
            with eng.Fori(0, (B - 2 - tail) // RING) as r:
                for k in range(RING):
                    step((r, 2 + k), None, None)
            for k in range(B - tail, B):
                step((None, k), None, B - 1 - k)

        def early(first, d):
            return first is not None and first < d

        def late(last, d):
            return last is not None and last < d

        block = ctx.enter_context(nc.Block())

        @block.sync
        def _(sp):
            def load(c, t):
                sp.dma_start(img[:, slot(c), t, :], x_v[num(c), t]).then_inc(load_done[slot(c)][t], 16)

            load((None, 0), 0)
            load((None, 0), 1)
            n = 0
            for dst, src in (
                (group_sb[:], group_w.rearrange("j p m -> p j m")),
                (w1_sb[:], w1.rearrange("(t p) h -> p t h", p=P)),
                (w2_sb[:], w2.rearrange("(t p) h -> p t h", p=P)),
                (w3_sb[:], w3.rearrange("(t p) h -> p t h", p=P)),
                (bias_sb[:], biases),
                (part_sb[:], part_w),
                (up_sb[:], up_w),
            ):
                sp.dma_start(dst, src).then_inc(weights_in, 16)
                n += 1
            assert n == WEIGHT_DMAS
            for k in (1, 2):
                load((None, k), 0)
                load((None, k), 1)

            def store(c, t):
                sp.wait_ge(added, num(c) * CH + NCH * (t + 1))
                sp.dma_start(out_v[num(c), t], img[:, slot(c), t, :]).then_inc(store_done[slot(c)][t], 16)

            def reload(c, t, first):
                if first is None or first + 3 >= RING:
                    sp.wait_ge(store_done[slot(c)][t], landed(shifted(c, -RING)))
                load(c, t)

            def step(c, first, last):
                if not early(first, 2):
                    store(shifted(c, -2), 1)
                if not late(last, 3):
                    reload(shifted(c, 3), 0, first)
                if not early(first, 1):
                    store(shifted(c, -1), 0)
                if not late(last, 3):
                    reload(shifted(c, 3), 1, first)

            steps(sp, step, tail=2 + RING)
            store((None, B - 2), 1)
            store((None, B - 1), 0)
            store((None, B - 1), 1)
            for k in range(B - RING, B):
                for t in range(CT):
                    sp.wait_ge(store_done[k % RING][t], landed((None, k)))

        @block.vector
        def _(dve):
            def pool_blocks(c, t):
                dve.wait_ge(load_done[slot(c)][t], landed(c))
                nc.vector.tensor_reduce(
                    block_sum[:, slot(c), t, :].rearrange("p (a b) -> p a b", a=GRID),
                    img[:, slot(c), t, :].rearrange("p (a r b s) -> p a b r s", a=GRID, r=CELL, b=GRID),
                    AX.XY, ALU.add).then_inc(pooled, 1)

            def channel_sums(c):
                dve.wait_ge(pooled, num(c) * CT + CT)
                nc.vector.tensor_reduce(chan_sum[:, slot(c), :], block_sum[:, slot(c), :, :],
                                        AX.X, ALU.add).then_inc(summed, 1)

            def add(c, t):
                for q in range(NCH):
                    dve.wait_ge(up_made, num(c) * CH + t * NCH + q + 1)
                    pix = img[:, slot(c), t, q * CHUNK:(q + 1) * CHUNK]
                    nc.vector.scalar_tensor_tensor(out=pix, in0=pix, scalar=b3_sb[:, t:t + 1],
                                                   in1=up_ps[:, q % 2, :], op0=ALU.add,
                                                   op1=ALU.add).then_inc(added, 1)

            nc.vector.memset(half_pow[:], -0.5).then_inc(consts_set, 1)
            nc.vector.memset(eps64[:], AREA * AREA * EPS).then_inc(consts_set, 1)
            nc.vector.memset(neigh[:], 0.0).then_inc(consts_set, 1)
            pool_blocks((None, 0), 0)
            pool_blocks((None, 0), 1)
            channel_sums((None, 0))
            dve.wait_ge(weights_in, 16 * WEIGHT_DMAS)

            def step(c, first, last):
                if not early(first, 2):
                    add(shifted(c, -2), 1)
                if not late(last, 1):
                    pool_blocks(shifted(c, 1), 0)
                if not early(first, 1):
                    add(shifted(c, -1), 0)
                if not late(last, 1):
                    pool_blocks(shifted(c, 1), 1)
                    channel_sums(shifted(c, 1))

            steps(dve, step)
            add((None, B - 2), 1)
            add((None, B - 1), 0)
            add((None, B - 1), 1)

        @block.tensor
        def _(pe):
            def shift(c):
                for t in range(CT):
                    pe.wait_ge(load_done[slot(c)][t], landed(c))
                if c[0] is not None or c[1] > 1:
                    pe.wait_ge(first_read, num(c) - 1)
                elif c[1] == 1:
                    pe.wait_ge(shift_read, 1)
                nc.tensor.matmul(small_ps[:, SHF:SHF + CT], group_sb[:, 0, :], img[:, slot(c), :, 0],
                                 start=True, stop=True).then_inc(shift_made, 1)

            def group_moments(c, last):
                pe.wait_ge(summed, num(c) + 1)
                pe.wait_ge(squared, num(c) * 4 + 4)
                if not late(last, 1):
                    pe.wait_ge(shift_read, num(c) + 2)
                nc.tensor.matmul(small_ps[:, MOM:MOM + CT], group_sb[:, 0, :], chan_sum[:, slot(c), :],
                                 start=True, stop=True)
                for part in range(2):
                    mm = nc.tensor.matmul(small_ps[:, MOM + CT:MOM + 2 * CT], group_sb[:, 1, :],
                                          sq_sum[:, slot(c), :, part], start=(part == 0), stop=(part == 1))
                mm.then_inc(moments_made, 1)

            def first_layer(c):
                pe.wait_ge(stat_steps, num(c) * STATS + STATS)
                for which in range(2):
                    for m in range(HT):
                        col = AB + (which * HT + m) * POS
                        for k in range(CT):
                            mm = nc.tensor.matmul(small_ps[:, col:col + POS],
                                                  w1_sb[:, which * CT + k, m * P:(m + 1) * P],
                                                  norm[:, k, :], start=(k == 0), stop=(k == CT - 1))
                mm.then_inc(ab_made, 1)

            def second_layer(c, q):
                m, n = q // 2, q % 2
                if q == 0:
                    pe.wait_ge(h1_ready, num(c) * HT + HT)
                if q >= 2 or c[0] is not None or c[1] > 0:
                    pe.wait_ge(h2_ready, num(c) * 4 + q - 1)
                for k in range(HT):
                    mm = nc.tensor.matmul(l2_ps[:, n, 0:QN], w2_sb[:, k, m * P:(m + 1) * P],
                                          h1[:, k, n * QN:(n + 1) * QN], start=(k == 0), stop=(k == HT - 1))
                mm.then_inc(l2_made, 1)

            def last_layer(c, half):
                if half == 0:
                    pe.wait_ge(fold_steps, num(c) * FOLDS + FOLDS)
                    if c[0] is not None or c[1] > 0:
                        pe.wait_ge(agg_read, num(c) * 2)
                for k in range(HT):
                    mm = nc.tensor.matmul(agg_ps[0:KUP, half * C:(half + 1) * C],
                                          nb_sum[:, k, half].rearrange("p a n -> p (a n)"),
                                          w3_sb[:, k, :], start=(k == 0), stop=(k == HT - 1))
                if half == HALVES - 1:
                    mm.then_inc(agg_made, 1)

            def upsample(c, t, q):
                if t == 0 and q == 0:
                    pe.wait_ge(stack_made, num(c) + 1)
                if c[0] is not None or c[1] > 0 or t * NCH + q >= 2:
                    pe.wait_ge(added, num(c) * CH + t * NCH + q - 1)
                half = q * HALVES // NCH
                for n in range(CHUNK // 512):
                    pix = q * CHUNK + n * 512
                    mm = nc.tensor.matmul(up_ps[:, q % 2, n * 512:(n + 1) * 512],
                                          stack[:, slot(c), half * C + t * P:half * C + (t + 1) * P],
                                          up_sb[:, pix:pix + 512], start=True, stop=True)
                mm.then_inc(up_made, 1)

            pe.wait_ge(weights_in, 16 * WEIGHT_DMAS)
            shift((None, 0))
            shift((None, 1))

            def step(c, first, last):
                prev, prev2 = shifted(c, -1), shifted(c, -2)
                group_moments(c, last)
                if not early(first, 2):
                    upsample(prev2, 1, 2)
                if not early(first, 1):
                    last_layer(prev, 0)
                if not early(first, 2):
                    upsample(prev2, 1, 3)
                if not early(first, 1):
                    last_layer(prev, 1)
                first_layer(c)
                if not early(first, 1):
                    for q in range(NCH):
                        upsample(prev, 0, q)
                for q in range(4):
                    second_layer(c, q)
                if not late(last, 2):
                    shift(shifted(c, 2))
                if not early(first, 1):
                    upsample(prev, 1, 0)
                    upsample(prev, 1, 1)

            steps(pe, step)
            upsample((None, B - 2), 1, 2)
            upsample((None, B - 2), 1, 3)
            last_layer((None, B - 1), 0)
            last_layer((None, B - 1), 1)
            for t in range(CT):
                for q in range(NCH):
                    upsample((None, B - 1), t, q)

        @block.scalar
        def _(act):
            def read_shift(c):
                act.wait_ge(shift_made, num(c) + 1)
                nc.scalar.mul(shift64[:, slot(c), :], small_ps[:, SHF:SHF + CT], -AREA * AREA) \
                    .then_inc(shift_read, 1)

            def squares(c, t, part):
                if t == 0 and part == 0:
                    act.wait_ge(shift_read, num(c) + 1)
                if part == 0:
                    act.wait_ge(load_done[slot(c)][t], landed(c))
                if t or part or c[0] is not None or c[1] > 0:
                    act.wait_ge(squared, num(c) * 4 + t * 2 + part)
                nc.scalar.activation(junk[:], img[:, slot(c), t, part * SQ:(part + 1) * SQ], ACT.Square,
                                           bias=shift64[:, slot(c), t:t + 1], scale=-64.0,
                                           accum_out=sq_sum[:, slot(c), t, part:part + 1]) \
                    .then_inc(squared, 1)

            def read_moments(c):
                act.wait_ge(moments_made, num(c) + 1)
                if c[0] is not None or c[1] > 0:
                    act.wait_ge(stat_steps, num(c) * STATS)
                nc.scalar.copy(moments[:].rearrange("p a t -> p (a t)"), small_ps[:, MOM:MOM + 2 * CT]) \
                    .then_inc(moments_read, 1)

            def read_first_layer(c):
                act.wait_ge(ab_made, num(c) + 1)
                if c[0] is not None or c[1] > 0:
                    act.wait_ge(pairs_made, num(c) * HT)
                inner = neigh[:].rearrange("p m (i j) -> p m i j", i=PADG)[:, :, 1:1 + GRID, 1:1 + GRID]
                nc.scalar.copy(centre[:].rearrange("p m n -> p (m n)"), small_ps[:, AB:AB + HT * POS])
                nc.scalar.copy(inner, small_ps[:, AB + HT * POS:AB + 2 * HT * POS]
                               .rearrange("p (m i j) -> p m i j", m=HT, i=GRID)).then_inc(first_read, 1)

            def relu1(c, m):
                act.wait_ge(pairs_made, num(c) * HT + m + 1)
                nc.scalar.activation(h1[:, m, :], h1[:, m, :], ACT.Relu, bias=b1_sb[:, m:m + 1]) \
                    .then_inc(h1_ready, 1)

            def relu2(c, q):
                m, n = q // 2, q % 2
                act.wait_ge(l2_made, num(c) * 4 + q + 1)
                if q == 0 and (c[0] is not None or c[1] > 0):
                    act.wait_ge(fold_steps, num(c) * FOLDS)
                nc.scalar.activation(h2[:, m, n * QN:(n + 1) * QN], l2_ps[:, n, 0:QN], ACT.Relu,
                                     bias=b2_sb[:, m:m + 1]).then_inc(h2_ready, 1)

            def read_agg(c):
                act.wait_ge(agg_made, num(c) + 1)
                if c[0] is not None or c[1] > 0:
                    act.wait_ge(rest_made, num(c))
                nc.scalar.mul(agg[:], agg_ps[0:KUP, :], 1.0 / NB).then_inc(agg_read, 1)
                nc.scalar.activation(high[:], agg_ps[0:KUP, :], ACT.Copy, scale=part_sb[:, 0:1]) \
                    .then_inc(agg_read, 1)

            def middle_part(c):
                act.wait_ge(rest_made, num(c) + 1)
                if c[0] is not None or c[1] > 0:
                    act.wait_ge(stack_made, num(c))
                nc.scalar.activation(mid[:], rest[:], ACT.Copy, scale=part_sb[:, 1:2]).then_inc(mid_made, 1)

            read_shift((None, 0))
            read_shift((None, 1))
            for t in range(CT):
                for part in range(2):
                    squares((None, 0), t, part)
            act.wait_ge(weights_in, 16 * WEIGHT_DMAS)
            act.wait_ge(consts_set, 3)

            def step(c, first, last):
                nxt, prev = shifted(c, 1), shifted(c, -1)
                more = not late(last, 1)
                read_moments(c)
                if more:
                    squares(nxt, 0, 0)
                if not early(first, 1):
                    read_agg(prev)
                    middle_part(prev)
                if more:
                    squares(nxt, 0, 1)
                read_first_layer(c)
                if more:
                    squares(nxt, 1, 0)
                relu1(c, 0)
                relu1(c, 1)
                for q in range(4):
                    relu2(c, q)
                if not late(last, 2):
                    read_shift(shifted(c, 2))
                if more:
                    squares(nxt, 1, 1)

            steps(act, step)
            read_agg((None, B - 1))
            middle_part((None, B - 1))

        @block.gpsimd
        def _(pool):
            def per_block(v):
                return bass.AP(v.tensor, v.offset, [v.ap[0], v.ap[1], [0, POS]])

            def statistics(c):
                done = num(c) * STATS
                neg_mean, second = moments[:, 0, :], moments[:, 1, :]
                delta, delta2, var, var_eps, rstd, bias = (st[:, i, :] for i in range(6))
                pool.wait_ge(moments_read, num(c) + 1)
                nc.gpsimd.tensor_tensor(delta, neg_mean, shift64[:, slot(c), :], ALU.add) \
                    .then_inc(stat_steps, 1)
                pool.wait_ge(stat_steps, done + 1)
                nc.gpsimd.tensor_tensor(delta2, delta, delta, ALU.mult).then_inc(stat_steps, 1)
                pool.wait_ge(stat_steps, done + 2)
                nc.gpsimd.tensor_tensor(var, second, delta2, ALU.subtract).then_inc(stat_steps, 1)
                pool.wait_ge(stat_steps, done + 3)
                nc.gpsimd.tensor_tensor(var_eps, var, eps64[:], ALU.add) \
                    .then_inc(stat_steps, 1)
                pool.wait_ge(stat_steps, done + 4)
                nc.gpsimd.tensor_tensor(rstd, var_eps, half_pow[:], ALU.pow).then_inc(stat_steps, 1)
                pool.wait_ge(stat_steps, done + 5)
                nc.gpsimd.tensor_tensor(bias, neg_mean, rstd, ALU.mult).then_inc(stat_steps, 1)
                pool.wait_ge(stat_steps, done + 6)
                if c[0] is not None or c[1] > 0:
                    pool.wait_ge(ab_made, num(c))
                pool.wait_ge(pooled, num(c) * CT + CT)
                nc.gpsimd.tensor_tensor(norm[:], block_sum[:, slot(c)], per_block(rstd), ALU.mult) \
                    .then_inc(stat_steps, 1)
                pool.wait_ge(stat_steps, done + 7)
                nc.gpsimd.tensor_tensor(norm[:], norm[:], per_block(bias), ALU.add).then_inc(stat_steps, 1)

            def pair_sums(c):
                pool.wait_ge(first_read, num(c) + 1)
                if c[0] is not None or c[1] > 0:
                    pool.wait_ge(l2_made, num(c) * 4)
                for m in range(HT):
                    cen = centre[:, m, :]
                    cen3 = bass.AP(cen.tensor, cen.offset, [cen.ap[0], [0, 3], [GRID, GRID], [1, GRID]])
                    for ki in range(3):
                        row = neigh[:, m, ki * PADG:]
                        row3 = bass.AP(row.tensor, row.offset, [row.ap[0], [1, 3], [PADG, GRID], [1, GRID]])
                        dst = h1[:, m, ki * 3 * POS:(ki + 1) * 3 * POS] \
                            .rearrange("p (k i j) -> p k i j", k=3, i=GRID)
                        ins = nc.gpsimd.tensor_tensor(dst, row3, cen3, ALU.add)
                    ins.then_inc(pairs_made, 1)

            def fold(c):
                done = num(c) * FOLDS
                pool.wait_ge(h2_ready, num(c) * 4 + 4)
                nc.gpsimd.tensor_tensor(fold4, h2[:, :, 0:4 * POS], h2[:, :, 4 * POS:8 * POS], ALU.add) \
                    .then_inc(fold_steps, 1)
                pool.wait_ge(fold_steps, done + 1)
                nc.gpsimd.tensor_tensor(fold2, fold4[:, :, 0:2 * POS], fold4[:, :, 2 * POS:], ALU.add) \
                    .then_inc(fold_steps, 1)
                pool.wait_ge(fold_steps, done + 2)
                nc.gpsimd.tensor_tensor(fold1, fold2[:, :, 0:POS], fold2[:, :, POS:], ALU.add) \
                    .then_inc(fold_steps, 1)
                pool.wait_ge(fold_steps, done + 3)
                if c[0] is not None or c[1] > 0:
                    pool.wait_ge(agg_made, num(c))
                for half in range(HALVES):
                    def reached(ap):
                        part = ap[:, :, half * (POS - KPOS):half * (POS - KPOS) + KPOS]
                        return bass.AP(part.tensor, part.offset, [part.ap[0], part.ap[1], [0, PARTS], [1, KPOS]])

                    ins = nc.gpsimd.tensor_tensor(nb_sum[:, :, half], reached(fold1),
                                                  reached(h2[:, :, 8 * POS:]), ALU.add)
                ins.then_inc(fold_steps, 1)

            def rest_part(c):
                pool.wait_ge(agg_read, num(c) * 2 + 2)
                if c[0] is not None or c[1] > 0:
                    pool.wait_ge(mid_made, num(c))
                    pool.wait_ge(stack_made, num(c))
                nc.gpsimd.tensor_tensor(rest[:], agg[:], high[:], ALU.subtract).then_inc(rest_made, 1)

            def stack_parts(c):
                pool.wait_ge(mid_made, num(c) + 1)
                nc.gpsimd.tensor_tensor(stack[:, slot(c), :], rest[:], mid[:], ALU.subtract) \
                    .then_inc(stack_made, 1)

            pool.wait_ge(consts_set, 3)

            def step(c, first, last):
                statistics(c)
                if not early(first, 1):
                    rest_part(shifted(c, -1))
                    stack_parts(shifted(c, -1))
                pair_sums(c)
                fold(c)

            steps(pool, step)
            rest_part((None, B - 1))
            stack_parts((None, B - 1))


WEIGHT_DMAS = 7


def kernel(x, L0_conv_w1, L0_conv_b1, L0_conv_w2, L0_conv_b2, L0_conv_w3, L0_conv_b3):
    import numpy as np
    import concourse.bacc as bacc
    from concourse.bass_utils import run_bass_kernel_spmd

    B, C, H, W = x.shape
    taps = np.zeros((GRID, H), np.float32)
    for o in range(H):
        centre = (o + 0.5) * GRID / H - 0.5
        low = int(np.floor(centre))
        for j, weight in ((low, low + 1 - centre), (low + 1, centre - low)):
            taps[min(max(j, 0), GRID - 1), o] += weight
    up_w = np.zeros((PARTS, REACH * GRID, H, W), np.float32)
    for half, first in ((0, 0), (1, GRID - REACH)):
        rows = slice(half * H // 2, (half + 1) * H // 2)
        for i in range(REACH):
            for j in range(GRID):
                up_w[:, i * GRID + j, rows] = taps[first + i, rows, None] * taps[j, None, :]
    up_w = up_w.reshape(PARTS * REACH * GRID, H * W).astype("bfloat16")
    per_group = C // GROUPS
    same = np.kron(np.eye(P // per_group), np.ones((per_group, per_group)))
    group_w = np.stack([-64.0 * same, same]).astype(np.float32) / np.float32(per_group * H * W)
    part = np.repeat(np.arange(PARTS), REACH * GRID)
    part_w = np.stack([(part >= 1) / NB, part >= 2], axis=1).astype(np.float32)

    biases = np.concatenate([np.asarray(b).reshape(-1, P).T for b in (L0_conv_b1, L0_conv_b2, L0_conv_b3)], axis=1)

    ins = {"x": x, "w1": L0_conv_w1, "w2": L0_conv_w2, "w3": L0_conv_w3, "biases": biases, "up_w": up_w, "group_w": group_w, "part_w": part_w}
    nc = bacc.Bacc("TRN2", target_bir_lowering=False, num_devices=1)
    arrays = {f"{k}_dram": np.ascontiguousarray(v) for k, v in ins.items()}
    args = [nc.dram_tensor(k, v.shape, mybir.dt.from_np(v.dtype), kind="ExternalInput").ap()
            for k, v in arrays.items()]
    args.append(nc.dram_tensor("out_dram", (B, C, H, W), F32, kind="ExternalOutput").ap())
    conv_preact_program(nc, *args)
    return run_bass_kernel_spmd(nc, [arrays], core_ids=[0]).results[0]["out_dram"]
```

```python
from contextlib import ExitStack

import concourse.bass as bass
from concourse import mybir


F32 = mybir.dt.float32
BF16 = mybir.dt.bfloat16
ALU = mybir.AluOpType
ACT = mybir.ActivationFunctionType
AX = mybir.AxisListType

P = 128
RING = 5
GROUPS = 32
EPS = 1e-5
GRID = 8
NB = 9
PARTS = 3
REACH = 5
CHUNK = 1024


def conv_preact_program(nc, x, w1, w2, w3, biases, up_w, group_w, part_w, out):
    B, C, H, W = x.shape
    HID = w2.shape[0]
    CT = C // P
    HT = HID // P
    PIX = H * W
    CELL = H // GRID
    POS = GRID * GRID
    AREA = CELL * CELL
    PAIRS = NB * POS
    HALVES = 2
    KPOS = REACH * GRID
    KUP = PARTS * KPOS
    NCH = PIX // CHUNK
    QN = PAIRS // 2
    SQ = PIX // 2
    PADG = GRID + 2
    assert CT == 2 and HT == 2 and B > RING and (B - 4) % RING == 0 and NCH == 4

    x_v = x.rearrange("b (t p) h w -> b t p (h w)", p=P)
    out_v = out.rearrange("b (t p) h w -> b t p (h w)", p=P)

    with ExitStack() as ctx:
        def sb(name, shape, dt=F32):
            return ctx.enter_context(nc.sbuf_tensor(name, shape, dt))

        def pb(name, shape, dt=F32):
            return ctx.enter_context(nc.psum_tensor(name, shape, dt))

        def sem(name):
            return ctx.enter_context(nc.semaphore(name))

        img = sb("img", [P, RING, CT, PIX])
        w1_sb = sb("w1_sb", [P, 2 * CT, HID])
        w2_sb = sb("w2_sb", [P, HT, HID])
        w3_sb = sb("w3_sb", [P, HT, C])
        bias_sb = sb("bias_sb", [P, HT + HT + CT])
        b1_sb, b2_sb, b3_sb = bias_sb[:, 0:HT], bias_sb[:, HT:2 * HT], bias_sb[:, 2 * HT:]
        up_sb = sb("up_sb", [KUP, PIX], BF16)
        group_sb = sb("group_sb", [P, 2, P])
        part_sb = sb("part_sb", [KUP, 2])
        half_pow = sb("half_pow", [P, CT])
        junk = sb("junk", [P, SQ], BF16)
        block_sum = sb("block_sum", [P, RING, CT, POS])
        chan_sum = sb("chan_sum", [P, RING, CT])
        shift64 = sb("shift64", [P, RING, CT])
        sq_sum = sb("sq_sum", [P, RING, CT, 2])
        moments = sb("moments", [P, 2, CT])
        st = sb("st", [P, 4, CT])
        norm = sb("norm", [P, CT, POS])
        centre = sb("centre", [P, HT, POS])
        neigh = sb("neigh", [P, HT, PADG * PADG])
        h1 = sb("h1", [P, HT, PAIRS])
        h2 = sb("h2", [P, HT, PAIRS])
        fold4 = h1[:, :, 0:4 * POS]
        fold2 = h1[:, :, 4 * POS:6 * POS]
        fold1 = h1[:, :, 6 * POS:7 * POS]
        nb_sum = sb("nb_sum", [P, HT, HALVES, PARTS, KPOS])
        agg = sb("agg", [KUP, HALVES * C])
        high = sb("high", [KUP, HALVES * C], BF16)
        rest = sb("rest", [KUP, HALVES * C])
        mid = sb("mid", [KUP, HALVES * C], BF16)
        stack = sb("stack", [KUP, RING, HALVES * C], BF16)

        up_ps = pb("up_ps", [P, 2, CHUNK])
        l2_ps = pb("l2_ps", [P, 2, 512])
        small_ps = pb("small_ps", [P, 512])
        agg_ps = l2_ps
        MOM, SHF, AB = 0, 8, 128

        weights_in = sem("weights_in")
        consts_set = sem("consts_set")
        load_done = [[sem(f"load_done_{s}_{t}") for t in range(CT)] for s in range(RING)]
        store_done = [[sem(f"store_done_{s}_{t}") for t in range(CT)] for s in range(RING)]
        pooled = sem("pooled")
        summed = sem("summed")
        added = sem("added")
        shift_made = sem("shift_made")
        moments_made = sem("moments_made")
        ab_made = sem("ab_made")
        shift_read = sem("shift_read")
        moments_read = sem("moments_read")
        first_read = sem("first_read")
        squared = sem("squared")
        stat_steps = sem("stat_steps")
        pairs_made = sem("pairs_made")
        h1_ready = sem("h1_ready")
        l2_made = sem("l2_made")
        h2_ready = sem("h2_ready")
        fold_steps = sem("fold_steps")
        agg_made = sem("agg_made")
        agg_read = sem("agg_read")
        rest_made = sem("rest_made")
        mid_made = sem("mid_made")
        stack_made = sem("stack_made")
        up_made = sem("up_made")

        STATS, FOLDS = 6, 8
        CH = CT * NCH

        def num(c):
            return c[0] * RING + c[1] if c[0] is not None else c[1]

        def shifted(c, d):
            return (c[0], c[1] + d)

        def slot(c):
            return c[1] % RING

        def landed(c):
            passes = c[1] // RING + 1
            return 16 * (c[0] + passes) if c[0] is not None else 16 * passes

        def steps(eng, step, tail=2):
            for k in range(2):
                step((None, k), k, None)
            with eng.Fori(0, (B - 2 - tail) // RING) as r:
                for k in range(RING):
                    step((r, 2 + k), None, None)
            for k in range(B - tail, B):
                step((None, k), None, B - 1 - k)

        def early(first, d):
            return first is not None and first < d

        def late(last, d):
            return last is not None and last < d

        block = ctx.enter_context(nc.Block())

        @block.sync
        def _(sp):
            def load(c, t):
                sp.dma_start(img[:, slot(c), t, :], x_v[num(c), t]).then_inc(load_done[slot(c)][t], 16)

            load((None, 0), 0)
            load((None, 0), 1)
            n = 0
            for dst, src in (
                (group_sb[:], group_w.rearrange("j p m -> p j m")),
                (w1_sb[:], w1.rearrange("(t p) h -> p t h", p=P)),
                (w2_sb[:], w2.rearrange("(t p) h -> p t h", p=P)),
                (w3_sb[:], w3.rearrange("(t p) h -> p t h", p=P)),
                (bias_sb[:], biases),
                (part_sb[:], part_w),
                (up_sb[:], up_w),
            ):
                sp.dma_start(dst, src).then_inc(weights_in, 16)
                n += 1
            assert n == WEIGHT_DMAS
            for k in (1, 2):
                load((None, k), 0)
                load((None, k), 1)

            def store(c, t):
                sp.wait_ge(added, num(c) * CH + NCH * (t + 1))
                sp.dma_start(out_v[num(c), t], img[:, slot(c), t, :]).then_inc(store_done[slot(c)][t], 16)

            def reload(c, t, first):
                if first is None or first + 3 >= RING:
                    sp.wait_ge(store_done[slot(c)][t], landed(shifted(c, -RING)))
                load(c, t)

            def step(c, first, last):
                if not early(first, 2):
                    store(shifted(c, -2), 1)
                if not late(last, 3):
                    reload(shifted(c, 3), 0, first)
                if not early(first, 1):
                    store(shifted(c, -1), 0)
                if not late(last, 3):
                    reload(shifted(c, 3), 1, first)

            steps(sp, step, tail=2 + RING)
            store((None, B - 2), 1)
            store((None, B - 1), 0)
            store((None, B - 1), 1)
            for k in range(B - RING, B):
                for t in range(CT):
                    sp.wait_ge(store_done[k % RING][t], landed((None, k)))

        @block.vector
        def _(dve):
            def pool_blocks(c, t):
                dve.wait_ge(load_done[slot(c)][t], landed(c))
                nc.vector.tensor_reduce(
                    block_sum[:, slot(c), t, :].rearrange("p (a b) -> p a b", a=GRID),
                    img[:, slot(c), t, :].rearrange("p (a r b s) -> p a b r s", a=GRID, r=CELL, b=GRID),
                    AX.XY, ALU.add).then_inc(pooled, 1)

            def channel_sums(c):
                dve.wait_ge(pooled, num(c) * CT + CT)
                nc.vector.tensor_reduce(chan_sum[:, slot(c), :], block_sum[:, slot(c), :, :],
                                        AX.X, ALU.add).then_inc(summed, 1)

            def add(c, t):
                for q in range(NCH):
                    dve.wait_ge(up_made, num(c) * CH + t * NCH + q + 1)
                    pix = img[:, slot(c), t, q * CHUNK:(q + 1) * CHUNK]
                    nc.vector.scalar_tensor_tensor(out=pix, in0=pix, scalar=b3_sb[:, t:t + 1],
                                                   in1=up_ps[:, q % 2, :], op0=ALU.add,
                                                   op1=ALU.add).then_inc(added, 1)

            nc.vector.memset(half_pow[:], -0.5).then_inc(consts_set, 1)
            nc.vector.memset(neigh[:], 0.0).then_inc(consts_set, 1)
            pool_blocks((None, 0), 0)
            pool_blocks((None, 0), 1)
            channel_sums((None, 0))
            dve.wait_ge(weights_in, 16 * WEIGHT_DMAS)

            def step(c, first, last):
                if not early(first, 2):
                    add(shifted(c, -2), 1)
                if not late(last, 1):
                    pool_blocks(shifted(c, 1), 0)
                if not early(first, 1):
                    add(shifted(c, -1), 0)
                if not late(last, 1):
                    pool_blocks(shifted(c, 1), 1)
                    channel_sums(shifted(c, 1))

            steps(dve, step)
            add((None, B - 2), 1)
            add((None, B - 1), 0)
            add((None, B - 1), 1)

        @block.tensor
        def _(pe):
            def shift(c):
                for t in range(CT):
                    pe.wait_ge(load_done[slot(c)][t], landed(c))
                if c[0] is not None or c[1] > 1:
                    pe.wait_ge(first_read, num(c) - 1)
                elif c[1] == 1:
                    pe.wait_ge(shift_read, 1)
                nc.tensor.matmul(small_ps[:, SHF:SHF + CT], group_sb[:, 0, :], img[:, slot(c), :, 0],
                                 start=True, stop=True).then_inc(shift_made, 1)

            def group_moments(c, last):
                pe.wait_ge(summed, num(c) + 1)
                pe.wait_ge(squared, num(c) * 4 + 4)
                if not late(last, 1):
                    pe.wait_ge(shift_read, num(c) + 2)
                nc.tensor.matmul(small_ps[:, MOM:MOM + CT], group_sb[:, 0, :], chan_sum[:, slot(c), :],
                                 start=True, stop=True)
                for part in range(2):
                    mm = nc.tensor.matmul(small_ps[:, MOM + CT:MOM + 2 * CT], group_sb[:, 1, :],
                                          sq_sum[:, slot(c), :, part], start=(part == 0), stop=(part == 1))
                mm.then_inc(moments_made, 1)

            def first_layer(c):
                pe.wait_ge(stat_steps, num(c) * STATS + STATS)
                for which in range(2):
                    for m in range(HT):
                        col = AB + (which * HT + m) * POS
                        for k in range(CT):
                            mm = nc.tensor.matmul(small_ps[:, col:col + POS],
                                                  w1_sb[:, which * CT + k, m * P:(m + 1) * P],
                                                  norm[:, k, :], start=(k == 0), stop=(k == CT - 1))
                mm.then_inc(ab_made, 1)

            def second_layer(c, q):
                m, n = q // 2, q % 2
                if q == 0:
                    pe.wait_ge(h1_ready, num(c) * HT + HT)
                if q >= 2:
                    pe.wait_ge(h2_ready, num(c) * 4 + q - 1)
                elif c[0] is not None or c[1] > 0:
                    pe.wait_ge(agg_read, num(c) * HALVES + q - 1)
                for k in range(HT):
                    mm = nc.tensor.matmul(l2_ps[:, n, 0:QN], w2_sb[:, k, m * P:(m + 1) * P],
                                          h1[:, k, n * QN:(n + 1) * QN], start=(k == 0), stop=(k == HT - 1))
                mm.then_inc(l2_made, 1)

            def last_layer(c, half):
                if half == 0:
                    pe.wait_ge(fold_steps, num(c) * FOLDS + FOLDS)
                for k in range(HT):
                    mm = nc.tensor.matmul(agg_ps[0:KUP, half, 0:C], nb_sum[:, k, half].rearrange("p a n -> p (a n)"),
                                          w3_sb[:, k, :], start=(k == 0), stop=(k == HT - 1))
                mm.then_inc(agg_made, 1)

            def upsample(c, t, q):
                if t == 0 and q % (NCH // HALVES) == 0:
                    pe.wait_ge(stack_made, num(c) * HALVES + q * HALVES // NCH + 1)
                if c[0] is not None or c[1] > 0 or t * NCH + q >= 2:
                    pe.wait_ge(added, num(c) * CH + t * NCH + q - 1)
                half = q * HALVES // NCH
                for n in range(CHUNK // 512):
                    pix = q * CHUNK + n * 512
                    mm = nc.tensor.matmul(up_ps[:, q % 2, n * 512:(n + 1) * 512],
                                          stack[:, slot(c), half * C + t * P:half * C + (t + 1) * P],
                                          up_sb[:, pix:pix + 512], start=True, stop=True)
                mm.then_inc(up_made, 1)

            pe.wait_ge(weights_in, 16 * WEIGHT_DMAS)
            shift((None, 0))
            shift((None, 1))

            def step(c, first, last):
                prev, prev2 = shifted(c, -1), shifted(c, -2)
                group_moments(c, last)
                if not early(first, 2):
                    upsample(prev2, 1, 2)
                if not early(first, 1):
                    last_layer(prev, 0)
                if not early(first, 2):
                    upsample(prev2, 1, 3)
                if not early(first, 1):
                    last_layer(prev, 1)
                first_layer(c)
                if not early(first, 1):
                    for q in range(NCH):
                        upsample(prev, 0, q)
                for q in range(4):
                    second_layer(c, q)
                if not late(last, 2):
                    shift(shifted(c, 2))
                if not early(first, 1):
                    upsample(prev, 1, 0)
                    upsample(prev, 1, 1)

            steps(pe, step)
            upsample((None, B - 2), 1, 2)
            upsample((None, B - 2), 1, 3)
            last_layer((None, B - 1), 0)
            last_layer((None, B - 1), 1)
            for t in range(CT):
                for q in range(NCH):
                    upsample((None, B - 1), t, q)

        @block.scalar
        def _(act):
            def read_shift(c):
                act.wait_ge(shift_made, num(c) + 1)
                nc.scalar.mul(shift64[:, slot(c), :], small_ps[:, SHF:SHF + CT], -AREA * AREA) \
                    .then_inc(shift_read, 1)

            def squares(c, t, part):
                if t == 0 and part == 0:
                    act.wait_ge(shift_read, num(c) + 1)
                if part == 0:
                    act.wait_ge(load_done[slot(c)][t], landed(c))
                if t or part or c[0] is not None or c[1] > 0:
                    act.wait_ge(squared, num(c) * 4 + t * 2 + part)
                nc.scalar.activation(junk[:], img[:, slot(c), t, part * SQ:(part + 1) * SQ], ACT.Square,
                                           bias=shift64[:, slot(c), t:t + 1], scale=-64.0,
                                           accum_out=sq_sum[:, slot(c), t, part:part + 1]) \
                    .then_inc(squared, 1)

            def read_moments(c):
                act.wait_ge(moments_made, num(c) + 1)
                if c[0] is not None or c[1] > 0:
                    act.wait_ge(stat_steps, num(c) * STATS)
                nc.scalar.copy(moments[:, 0, :], small_ps[:, MOM:MOM + CT]).then_inc(moments_read, 1)
                nc.scalar.activation(moments[:, 1, :], small_ps[:, MOM + CT:MOM + 2 * CT], ACT.Copy,
                                     bias=AREA * AREA * EPS).then_inc(moments_read, 1)

            def read_first_layer(c):
                act.wait_ge(ab_made, num(c) + 1)
                if c[0] is not None or c[1] > 0:
                    act.wait_ge(pairs_made, num(c) * HT)
                inner = neigh[:].rearrange("p m (i j) -> p m i j", i=PADG)[:, :, 1:1 + GRID, 1:1 + GRID]
                nc.scalar.copy(centre[:].rearrange("p m n -> p (m n)"), small_ps[:, AB:AB + HT * POS])
                nc.scalar.copy(inner, small_ps[:, AB + HT * POS:AB + 2 * HT * POS]
                               .rearrange("p (m i j) -> p m i j", m=HT, i=GRID)).then_inc(first_read, 1)

            def relu1(c, m):
                act.wait_ge(pairs_made, num(c) * HT + m + 1)
                nc.scalar.activation(h1[:, m, :], h1[:, m, :], ACT.Relu, bias=b1_sb[:, m:m + 1]) \
                    .then_inc(h1_ready, 1)

            def relu2(c, q):
                m, n = q // 2, q % 2
                act.wait_ge(l2_made, num(c) * 4 + q + 1)
                if q == 0 and (c[0] is not None or c[1] > 0):
                    act.wait_ge(fold_steps, num(c) * FOLDS)
                nc.scalar.activation(h2[:, m, n * QN:(n + 1) * QN], l2_ps[:, n, 0:QN], ACT.Relu,
                                     bias=b2_sb[:, m:m + 1]).then_inc(h2_ready, 1)

            def read_agg(c, half):
                n = num(c) * HALVES + half
                act.wait_ge(agg_made, n + 1)
                if c[0] is not None or c[1] > 0:
                    act.wait_ge(rest_made, num(c) * HALVES + half - 1)
                cols = slice(half * C, (half + 1) * C)
                nc.scalar.mul(agg[:, cols], agg_ps[0:KUP, half, 0:C], 1.0 / NB)
                nc.scalar.activation(high[:, cols], agg_ps[0:KUP, half, 0:C], ACT.Copy, scale=part_sb[:, 0:1]) \
                    .then_inc(agg_read, 1)

            def middle_part(c, half):
                n = num(c) * HALVES + half
                act.wait_ge(rest_made, n + 1)
                if c[0] is not None or c[1] > 0:
                    act.wait_ge(stack_made, num(c) * HALVES + half - 1)
                cols = slice(half * C, (half + 1) * C)
                nc.scalar.activation(mid[:, cols], rest[:, cols], ACT.Copy, scale=part_sb[:, 1:2]) \
                    .then_inc(mid_made, 1)

            read_shift((None, 0))
            read_shift((None, 1))
            for t in range(CT):
                for part in range(2):
                    squares((None, 0), t, part)
            act.wait_ge(weights_in, 16 * WEIGHT_DMAS)
            act.wait_ge(consts_set, 2)

            def step(c, first, last):
                nxt, prev = shifted(c, 1), shifted(c, -1)
                more = not late(last, 1)
                read_moments(c)
                if more:
                    squares(nxt, 0, 0)
                    squares(nxt, 0, 1)
                if not early(first, 1):
                    read_agg(prev, 0)
                    middle_part(prev, 0)
                    read_agg(prev, 1)
                    read_first_layer(c)
                    middle_part(prev, 1)
                else:
                    read_first_layer(c)
                if more:
                    squares(nxt, 1, 0)
                relu1(c, 0)
                relu1(c, 1)
                if more:
                    squares(nxt, 1, 1)
                for q in range(4):
                    relu2(c, q)
                if not late(last, 2):
                    read_shift(shifted(c, 2))

            steps(act, step)
            for half in range(HALVES):
                read_agg((None, B - 1), half)
                middle_part((None, B - 1), half)

        @block.gpsimd
        def _(pool):
            def per_block(v):
                return bass.AP(v.tensor, v.offset, [v.ap[0], v.ap[1], [0, POS]])

            def statistics(c):
                done = num(c) * STATS
                neg_mean, second = moments[:, 0, :], moments[:, 1, :]
                delta, delta2, var, rstd = (st[:, i, :] for i in range(4))
                pool.wait_ge(moments_read, num(c) * 2 + 1)
                nc.gpsimd.tensor_tensor(delta, neg_mean, shift64[:, slot(c), :], ALU.add) \
                    .then_inc(stat_steps, 1)
                pool.wait_ge(stat_steps, done + 1)
                nc.gpsimd.tensor_tensor(delta2, delta, delta, ALU.mult).then_inc(stat_steps, 1)
                pool.wait_ge(stat_steps, done + 2)
                pool.wait_ge(moments_read, num(c) * 2 + 2)
                nc.gpsimd.tensor_tensor(var, second, delta2, ALU.subtract).then_inc(stat_steps, 1)
                if c[0] is not None or c[1] > 0:
                    pool.wait_ge(ab_made, num(c))
                pool.wait_ge(pooled, num(c) * CT + CT)
                nc.gpsimd.tensor_tensor(norm[:], block_sum[:, slot(c)], per_block(neg_mean), ALU.add) \
                    .then_inc(stat_steps, 1)
                pool.wait_ge(stat_steps, done + 3)
                nc.gpsimd.tensor_tensor(rstd, var, half_pow[:], ALU.pow).then_inc(stat_steps, 1)
                pool.wait_ge(stat_steps, done + 5)
                nc.gpsimd.tensor_tensor(norm[:], norm[:], per_block(rstd), ALU.mult).then_inc(stat_steps, 1)

            def pair_sums(c):
                pool.wait_ge(first_read, num(c) + 1)
                if c[0] is not None or c[1] > 0:
                    pool.wait_ge(l2_made, num(c) * 4)
                for m in range(HT):
                    cen = centre[:, m, :]
                    cen3 = bass.AP(cen.tensor, cen.offset, [cen.ap[0], [0, 3], [GRID, GRID], [1, GRID]])
                    for ki in range(3):
                        row = neigh[:, m, ki * PADG:]
                        row3 = bass.AP(row.tensor, row.offset, [row.ap[0], [1, 3], [PADG, GRID], [1, GRID]])
                        dst = h1[:, m, ki * 3 * POS:(ki + 1) * 3 * POS] \
                            .rearrange("p (k i j) -> p k i j", k=3, i=GRID)
                        ins = nc.gpsimd.tensor_tensor(dst, row3, cen3, ALU.add)
                    ins.then_inc(pairs_made, 1)

            def fold(c, m):
                done = num(c) * FOLDS + m * FOLDS // HT
                pool.wait_ge(h2_ready, num(c) * 4 + 2 * m + 2)
                if m == 0:
                    pool.wait_ge(l2_made, num(c) * 4 + 4)
                nc.gpsimd.tensor_tensor(fold4[:, m], h2[:, m, 0:4 * POS], h2[:, m, 4 * POS:8 * POS], ALU.add) \
                    .then_inc(fold_steps, 1)
                pool.wait_ge(fold_steps, done + 1)
                nc.gpsimd.tensor_tensor(fold2[:, m], fold4[:, m, 0:2 * POS], fold4[:, m, 2 * POS:], ALU.add) \
                    .then_inc(fold_steps, 1)
                pool.wait_ge(fold_steps, done + 2)
                nc.gpsimd.tensor_tensor(fold1[:, m], fold2[:, m, 0:POS], fold2[:, m, POS:], ALU.add) \
                    .then_inc(fold_steps, 1)
                pool.wait_ge(fold_steps, done + 3)
                if c[0] is not None or c[1] > 0:
                    pool.wait_ge(agg_made, num(c))

                def reached(ap):
                    return bass.AP(ap.tensor, ap.offset, [ap.ap[0], [POS - KPOS, HALVES], [0, PARTS], [1, KPOS]])

                nc.gpsimd.tensor_tensor(nb_sum[:, m], reached(fold1[:, m]), reached(h2[:, m, 8 * POS:]),
                                        ALU.add).then_inc(fold_steps, 1)

            def rest_part(c, half):
                n = num(c) * HALVES + half
                pool.wait_ge(agg_read, n + 1)
                cols = slice(half * C, (half + 1) * C)
                if c[0] is not None or c[1] > 0:
                    pool.wait_ge(stack_made, num(c) * HALVES + half - 1)
                nc.gpsimd.tensor_tensor(rest[:, cols], agg[:, cols], high[:, cols], ALU.subtract) \
                    .then_inc(rest_made, 1)

            def stack_parts(c, half):
                n = num(c) * HALVES + half
                pool.wait_ge(mid_made, n + 1)
                cols = slice(half * C, (half + 1) * C)
                nc.gpsimd.tensor_tensor(stack[:, slot(c), cols], rest[:, cols], mid[:, cols], ALU.subtract) \
                    .then_inc(stack_made, 1)

            pool.wait_ge(consts_set, 2)

            def step(c, first, last):
                statistics(c)
                if not early(first, 1):
                    for half in range(HALVES):
                        rest_part(shifted(c, -1), half)
                        stack_parts(shifted(c, -1), half)
                pair_sums(c)
                fold(c, 0)
                fold(c, 1)

            steps(pool, step)
            for half in range(HALVES):
                rest_part((None, B - 1), half)
                stack_parts((None, B - 1), half)


WEIGHT_DMAS = 7


def kernel(x, L0_conv_w1, L0_conv_b1, L0_conv_w2, L0_conv_b2, L0_conv_w3, L0_conv_b3):
    import numpy as np
    import concourse.bacc as bacc
    from concourse.bass_utils import run_bass_kernel_spmd

    B, C, H, W = x.shape
    taps = np.zeros((GRID, H), np.float32)
    for o in range(H):
        centre = (o + 0.5) * GRID / H - 0.5
        low = int(np.floor(centre))
        for j, weight in ((low, low + 1 - centre), (low + 1, centre - low)):
            taps[min(max(j, 0), GRID - 1), o] += weight
    up_w = np.zeros((PARTS, REACH * GRID, H, W), np.float32)
    for half, first in ((0, 0), (1, GRID - REACH)):
        rows = slice(half * H // 2, (half + 1) * H // 2)
        for i in range(REACH):
            for j in range(GRID):
                up_w[:, i * GRID + j, rows] = taps[first + i, rows, None] * taps[j, None, :]
    up_w = up_w.reshape(PARTS * REACH * GRID, H * W).astype("bfloat16")
    per_group = C // GROUPS
    same = np.kron(np.eye(P // per_group), np.ones((per_group, per_group)))
    group_w = np.stack([-64.0 * same, same]).astype(np.float32) / np.float32(per_group * H * W)
    part = np.repeat(np.arange(PARTS), REACH * GRID)
    part_w = np.stack([(part >= 1) / NB, part >= 2], axis=1).astype(np.float32)

    biases = np.concatenate([np.asarray(b).reshape(-1, P).T for b in (L0_conv_b1, L0_conv_b2, L0_conv_b3)], axis=1)

    ins = {"x": x, "w1": L0_conv_w1, "w2": L0_conv_w2, "w3": L0_conv_w3, "biases": biases, "up_w": up_w, "group_w": group_w, "part_w": part_w}
    nc = bacc.Bacc("TRN2", target_bir_lowering=False, num_devices=1)
    arrays = {f"{k}_dram": np.ascontiguousarray(v) for k, v in ins.items()}
    args = [nc.dram_tensor(k, v.shape, mybir.dt.from_np(v.dtype), kind="ExternalInput").ap()
            for k, v in arrays.items()]
    args.append(nc.dram_tensor("out_dram", (B, C, H, W), F32, kind="ExternalOutput").ap())
    conv_preact_program(nc, *args)
    return run_bass_kernel_spmd(nc, [arrays], core_ids=[0]).results[0]["out_dram"]
```

```python
from contextlib import ExitStack

import concourse.bass as bass
from concourse import mybir


F32 = mybir.dt.float32
BF16 = mybir.dt.bfloat16
ALU = mybir.AluOpType
ACT = mybir.ActivationFunctionType
AX = mybir.AxisListType

P = 128
RING = 5
GROUPS = 32
EPS = 1e-5
GRID = 8
NB = 9
PARTS = 3
REACH = 5
CHUNK = 1024


def conv_preact_program(nc, x, w1, w2, w3, biases, up_w, group_w, part_w, out):
    B, C, H, W = x.shape
    HID = w2.shape[0]
    CT = C // P
    HT = HID // P
    PIX = H * W
    CELL = H // GRID
    POS = GRID * GRID
    AREA = CELL * CELL
    PAIRS = NB * POS
    HALVES = 2
    KPOS = REACH * GRID
    KUP = PARTS * KPOS
    NCH = PIX // CHUNK
    QN = PAIRS // 2
    SQ = PIX // 2
    PADG = GRID + 2
    assert CT == 2 and HT == 2 and B > RING and (B - 4) % RING == 0 and NCH == 4

    x_v = x.rearrange("b (t p) h w -> (b t) p (h w)", p=P)
    out_v = out.rearrange("b (t p) h w -> (b t) p (h w)", p=P)

    with ExitStack() as ctx:
        def sb(name, shape, dt=F32):
            return ctx.enter_context(nc.sbuf_tensor(name, shape, dt))

        def pb(name, shape, dt=F32):
            return ctx.enter_context(nc.psum_tensor(name, shape, dt))

        def sem(name):
            return ctx.enter_context(nc.semaphore(name))

        img = sb("img", [P, RING, CT, PIX])
        w1_sb = sb("w1_sb", [P, 2 * CT, HID])
        w2_sb = sb("w2_sb", [P, HT, HID])
        w3_sb = sb("w3_sb", [P, HT, C])
        bias_sb = sb("bias_sb", [P, HT + HT + CT])
        b1_sb, b2_sb, b3_sb = bias_sb[:, 0:HT], bias_sb[:, HT:2 * HT], bias_sb[:, 2 * HT:]
        up_sb = sb("up_sb", [KUP, PIX], BF16)
        group_sb = sb("group_sb", [P, 2, P])
        part_sb = sb("part_sb", [KUP, 2])
        half_pow = sb("half_pow", [P, CT])
        junk = sb("junk", [P, SQ], BF16)
        block_sum = sb("block_sum", [P, RING, CT, POS])
        chan_sum = sb("chan_sum", [P, RING, CT])
        shift64 = sb("shift64", [P, RING, CT])
        sq_sum = sb("sq_sum", [P, RING, CT, 2])
        moments = sb("moments", [P, 2, CT])
        st = sb("st", [P, 4, CT])
        norm = sb("norm", [P, CT, POS])
        centre = sb("centre", [P, HT, POS])
        neigh = sb("neigh", [P, HT, PADG * PADG])
        h1 = sb("h1", [P, HT, PAIRS])
        h2 = sb("h2", [P, HT, PAIRS])
        nb_sum = sb("nb_sum", [P, HT, HALVES, PARTS, KPOS])
        agg = sb("agg", [KUP, HALVES * C])
        high = sb("high", [KUP, HALVES * C], BF16)
        rest = sb("rest", [KUP, HALVES * C])
        mid = sb("mid", [KUP, HALVES * C], BF16)
        stack = sb("stack", [KUP, RING, HALVES * C], BF16)

        up_ps = pb("up_ps", [P, 2, CHUNK])
        l2_ps = pb("l2_ps", [P, 2, 512])
        small_ps = pb("small_ps", [P, 512])
        shift_ps = pb("shift_ps", [P, 512])
        agg_ps = l2_ps
        MOM, AB = 0, 128

        group_in = sem("group_in")
        weights_in = sem("weights_in")
        consts_set = sem("consts_set")
        load_done = [[sem(f"load_done_{s}_{t}") for t in range(CT)] for s in range(RING)]
        store_done = [[sem(f"store_done_{s}_{t}") for t in range(CT)] for s in range(RING)]
        pooled = sem("pooled")
        summed = sem("summed")
        added = sem("added")
        shift_made = sem("shift_made")
        moments_made = sem("moments_made")
        ab_made = sem("ab_made")
        shift_read = sem("shift_read")
        moments_read = sem("moments_read")
        first_read = sem("first_read")
        squared = sem("squared")
        stat_steps = sem("stat_steps")
        pairs_made = sem("pairs_made")
        h1_ready = sem("h1_ready")
        l2_made = sem("l2_made")
        h2_ready = sem("h2_ready")
        fold_steps = sem("fold_steps")
        agg_made = sem("agg_made")
        agg_read = sem("agg_read")
        rest_made = sem("rest_made")
        mid_made = sem("mid_made")
        stack_made = sem("stack_made")
        up_made = sem("up_made")

        STATS, FOLDS = 6, 8
        CH = CT * NCH

        def num(c):
            return c[0] * RING + c[1] if c[0] is not None else c[1]

        def shifted(c, d):
            return (c[0], c[1] + d)

        def slot(c):
            return c[1] % RING

        def landed(c):
            passes = c[1] // RING + 1
            return 16 * (c[0] + passes) if c[0] is not None else 16 * passes

        def steps(eng, step, head=2, tail=2):
            for k in range(head):
                step((None, k), k, None)
            with eng.Fori(0, (B - head - tail) // RING) as r:
                for k in range(RING):
                    step((r, head + k), None, None)
            for k in range(B - tail, B):
                step((None, k), None, B - 1 - k)

        def early(first, d):
            return first is not None and first < d

        def late(last, d):
            return last is not None and last < d

        block = ctx.enter_context(nc.Block())

        @block.sync
        def _(sp):
            def load(c, t):
                sp.dma_start(img[:, slot(c), t, :], x_v[num(c) * CT + t]).then_inc(load_done[slot(c)][t], 16)

            sp.dma_start(group_sb[:], group_w.rearrange("j p m -> p j m")).then_inc(group_in, 16)
            for t in range(CT):
                load((None, 0), t)
            n = 0
            for dst, src in (
                (w1_sb[:], w1.rearrange("(t p) h -> p t h", p=P)),
                (w2_sb[:], w2.rearrange("(t p) h -> p t h", p=P)),
                (w3_sb[:], w3.rearrange("(t p) h -> p t h", p=P)),
                (bias_sb[:], biases),
                (part_sb[:], part_w),
                (up_sb[:], up_w),
            ):
                sp.dma_start(dst, src).then_inc(weights_in, 16)
                n += 1
            assert n == WEIGHT_DMAS
            for k in range(1, RING):
                for t in range(CT):
                    load((None, k), t)

            def store(c, t):
                sp.wait_ge(added, num(c) * CH + NCH * (t + 1))
                sp.dma_start(out_v[num(c) * CT + t], img[:, slot(c), t, :]).then_inc(store_done[slot(c)][t], 16)

            def reload(c, t):
                sp.wait_ge(store_done[slot(c)][t], landed(shifted(c, -RING)))
                load(c, t)

            def step(c, first, last):
                if not early(first, 2):
                    store(shifted(c, -2), 0)
                if not early(first, 3) and not late(last, 2):
                    reload(shifted(c, 2), 1)
                if not early(first, 2):
                    store(shifted(c, -2), 1)
                if not early(first, 2) and not late(last, 3):
                    reload(shifted(c, 3), 0)

            steps(sp, step, head=2 + RING, tail=2 + RING)
            for k in (B - 2, B - 1):
                for t in range(CT):
                    store((None, k), t)
            for k in range(B - RING, B):
                for t in range(CT):
                    sp.wait_ge(store_done[k % RING][t], landed((None, k)))

        @block.vector
        def _(dve):
            def pool_blocks(c, t):
                dve.wait_ge(load_done[slot(c)][t], landed(c))
                nc.vector.tensor_reduce(
                    block_sum[:, slot(c), t, :].rearrange("p (a b) -> p a b", a=GRID),
                    img[:, slot(c), t, :].rearrange("p (a r b s) -> p a b r s", a=GRID, r=CELL, b=GRID),
                    AX.XY, ALU.add).then_inc(pooled, 1)

            def channel_sums(c):
                dve.wait_ge(pooled, num(c) * CT + CT)
                nc.vector.tensor_reduce(chan_sum[:, slot(c), :], block_sum[:, slot(c), :, :],
                                        AX.X, ALU.add).then_inc(summed, 1)

            def add(c, t):
                for q in range(NCH):
                    dve.wait_ge(up_made, num(c) * CH + t * NCH + q + 1)
                    pix = img[:, slot(c), t, q * CHUNK:(q + 1) * CHUNK]
                    nc.vector.scalar_tensor_tensor(out=pix, in0=pix, scalar=b3_sb[:, t:t + 1],
                                                   in1=up_ps[:, q % 2, :], op0=ALU.add,
                                                   op1=ALU.add).then_inc(added, 1)

            nc.vector.memset(half_pow[:], -0.5).then_inc(consts_set, 1)
            nc.vector.memset(neigh[:], 0.0).then_inc(consts_set, 1)
            pool_blocks((None, 0), 0)
            pool_blocks((None, 0), 1)
            channel_sums((None, 0))
            dve.wait_ge(weights_in, 16 * WEIGHT_DMAS)

            def step(c, first, last):
                if not early(first, 2):
                    add(shifted(c, -2), 0)
                    add(shifted(c, -2), 1)
                if not late(last, 1):
                    pool_blocks(shifted(c, 1), 0)
                    pool_blocks(shifted(c, 1), 1)
                    channel_sums(shifted(c, 1))

            steps(dve, step)
            for k in (B - 2, B - 1):
                for t in range(CT):
                    add((None, k), t)

        @block.tensor
        def _(pe):
            def shift(c, t):
                pe.wait_ge(load_done[slot(c)][t], landed(c))
                if c[0] is not None or c[1] > 0 or t > 0:
                    pe.wait_ge(shift_read, num(c) * CT + t)
                nc.tensor.matmul(shift_ps[:, t:t + 1], group_sb[:, 0, :], img[:, slot(c), t, 0:1],
                                 start=True, stop=True).then_inc(shift_made, 1)

            def group_moments(c):
                pe.wait_ge(summed, num(c) + 1)
                pe.wait_ge(squared, num(c) * 4 + 4)
                if c[0] is not None or c[1] > 0:
                    pe.wait_ge(first_read, num(c))
                nc.tensor.matmul(small_ps[:, MOM:MOM + CT], group_sb[:, 0, :], chan_sum[:, slot(c), :],
                                 start=True, stop=True)
                for part in range(2):
                    mm = nc.tensor.matmul(small_ps[:, MOM + CT:MOM + 2 * CT], group_sb[:, 1, :],
                                          sq_sum[:, slot(c), :, part], start=(part == 0), stop=(part == 1))
                mm.then_inc(moments_made, 1)

            def first_layer(c, which):
                if which == 0:
                    if c[0] is None and c[1] == 0:
                        pe.wait_ge(weights_in, 16 * WEIGHT_DMAS)
                    pe.wait_ge(stat_steps, num(c) * STATS + STATS)
                for m in range(HT):
                    col = AB + (which * HT + m) * POS
                    for k in range(CT):
                        mm = nc.tensor.matmul(small_ps[:, col:col + POS],
                                              w1_sb[:, which * CT + k, m * P:(m + 1) * P],
                                              norm[:, k, :], start=(k == 0), stop=(k == CT - 1))
                if which == 1:
                    mm.then_inc(ab_made, 1)

            def second_layer(c, q):
                m, n = q // 2, q % 2
                if q == 0:
                    pe.wait_ge(h1_ready, num(c) * HT + HT)
                if q >= 2:
                    pe.wait_ge(h2_ready, num(c) * 4 + q - 1)
                elif c[0] is not None or c[1] > 0:
                    pe.wait_ge(agg_read, num(c) * HALVES + q - 1)
                for k in range(HT):
                    mm = nc.tensor.matmul(l2_ps[:, n, 0:QN], w2_sb[:, k, m * P:(m + 1) * P],
                                          h1[:, k, n * QN:(n + 1) * QN], start=(k == 0), stop=(k == HT - 1))
                mm.then_inc(l2_made, 1)

            def last_layer(c, half):
                if half == 0:
                    pe.wait_ge(fold_steps, num(c) * FOLDS + FOLDS)
                for k in range(HT):
                    mm = nc.tensor.matmul(agg_ps[0:KUP, half, 0:C], nb_sum[:, k, half].rearrange("p a n -> p (a n)"),
                                          w3_sb[:, k, :], start=(k == 0), stop=(k == HT - 1))
                mm.then_inc(agg_made, 1)

            def upsample(c, n):
                t, q = n // NCH, n % NCH
                if t == 0 and q % (NCH // HALVES) == 0:
                    pe.wait_ge(stack_made, num(c) * HALVES + q * HALVES // NCH + 1)
                if c[0] is not None or c[1] > 0 or n >= 2:
                    pe.wait_ge(added, num(c) * CH + n - 1)
                half = q * HALVES // NCH
                for b in range(CHUNK // 512):
                    pix = q * CHUNK + b * 512
                    mm = nc.tensor.matmul(up_ps[:, q % 2, b * 512:(b + 1) * 512],
                                          stack[:, slot(c), half * C + t * P:half * C + (t + 1) * P],
                                          up_sb[:, pix:pix + 512], start=True, stop=True)
                mm.then_inc(up_made, 1)

            pe.wait_ge(group_in, 16)
            shift((None, 0), 0)
            shift((None, 0), 1)

            def step(c, first, last):
                ups = [] if early(first, 2) else list(range(2, CH))

                def chunks(n):
                    for _ in range(min(n, len(ups))):
                        upsample(shifted(c, -2), ups.pop(0))

                prev = shifted(c, -1)
                if first == 2:
                    chunks(4)
                if not early(first, 1):
                    second_layer(prev, 2)
                    second_layer(prev, 3)
                group_moments(c)
                if not late(last, 1):
                    shift(shifted(c, 1), 0)
                if first != 2:
                    chunks(2)
                first_layer(c, 0)
                chunks(1)
                first_layer(c, 1)
                chunks(1)
                for half in range(HALVES):
                    if not early(first, 1):
                        last_layer(prev, half)
                    chunks(1)
                if not late(last, 1):
                    shift(shifted(c, 1), 1)
                second_layer(c, 0)
                second_layer(c, 1)
                if not early(first, 1):
                    upsample(prev, 0)
                    upsample(prev, 1)

            steps(pe, step, head=3, tail=1)
            second_layer((None, B - 1), 2)
            second_layer((None, B - 1), 3)
            for n in range(2, CH):
                if n >= CH - HALVES:
                    last_layer((None, B - 1), n - (CH - HALVES))
                upsample((None, B - 2), n)
            for n in range(CH):
                upsample((None, B - 1), n)

        @block.scalar
        def _(act):
            def read_shift(c, t):
                act.wait_ge(shift_made, num(c) * CT + t + 1)
                nc.scalar.mul(shift64[:, slot(c), t:t + 1], shift_ps[:, t:t + 1], -AREA * AREA) \
                    .then_inc(shift_read, 1)

            def squares(c, t, part):
                if part == 0:
                    act.wait_ge(shift_read, num(c) * CT + t + 1)
                    act.wait_ge(load_done[slot(c)][t], landed(c))
                if t or part or c[0] is not None or c[1] > 0:
                    act.wait_ge(squared, num(c) * 4 + t * 2 + part)
                nc.scalar.activation(junk[:], img[:, slot(c), t, part * SQ:(part + 1) * SQ], ACT.Square,
                                           bias=shift64[:, slot(c), t:t + 1], scale=-64.0,
                                           accum_out=sq_sum[:, slot(c), t, part:part + 1]) \
                    .then_inc(squared, 1)

            def read_moments(c):
                act.wait_ge(moments_made, num(c) + 1)
                if c[0] is not None or c[1] > 0:
                    act.wait_ge(stat_steps, num(c) * STATS)
                nc.scalar.copy(moments[:, 0, :], small_ps[:, MOM:MOM + CT]).then_inc(moments_read, 1)
                nc.scalar.activation(moments[:, 1, :], small_ps[:, MOM + CT:MOM + 2 * CT], ACT.Copy,
                                     bias=AREA * AREA * EPS).then_inc(moments_read, 1)

            def read_first_layer(c):
                act.wait_ge(ab_made, num(c) + 1)
                if c[0] is not None or c[1] > 0:
                    act.wait_ge(pairs_made, num(c) * HT)
                inner = neigh[:].rearrange("p m (i j) -> p m i j", i=PADG)[:, :, 1:1 + GRID, 1:1 + GRID]
                nc.scalar.copy(centre[:].rearrange("p m n -> p (m n)"), small_ps[:, AB:AB + HT * POS])
                nc.scalar.copy(inner, small_ps[:, AB + HT * POS:AB + 2 * HT * POS]
                               .rearrange("p (m i j) -> p m i j", m=HT, i=GRID)).then_inc(first_read, 1)

            def relu1(c, m):
                if c[0] is None and c[1] == 0 and m == 0:
                    act.wait_ge(weights_in, 16 * WEIGHT_DMAS)
                act.wait_ge(pairs_made, num(c) * HT + m + 1)
                nc.scalar.activation(h1[:, m, :], h1[:, m, :], ACT.Relu, bias=b1_sb[:, m:m + 1]) \
                    .then_inc(h1_ready, 1)

            def relu2(c, q):
                m, n = q // 2, q % 2
                act.wait_ge(l2_made, num(c) * 4 + q + 1)
                if q == 0 and (c[0] is not None or c[1] > 0):
                    act.wait_ge(fold_steps, num(c) * FOLDS)
                nc.scalar.activation(h2[:, m, n * QN:(n + 1) * QN], l2_ps[:, n, 0:QN], ACT.Relu,
                                     bias=b2_sb[:, m:m + 1]).then_inc(h2_ready, 1)

            def read_agg(c, half):
                n = num(c) * HALVES + half
                act.wait_ge(agg_made, n + 1)
                if c[0] is not None or c[1] > 0:
                    act.wait_ge(rest_made, num(c) * HALVES + half - 1)
                cols = slice(half * C, (half + 1) * C)
                nc.scalar.mul(agg[:, cols], agg_ps[0:KUP, half, 0:C], 1.0 / NB)
                nc.scalar.activation(high[:, cols], agg_ps[0:KUP, half, 0:C], ACT.Copy, scale=part_sb[:, 0:1]) \
                    .then_inc(agg_read, 1)

            def middle_part(c, half):
                n = num(c) * HALVES + half
                act.wait_ge(rest_made, n + 1)
                if c[0] is not None or c[1] > 0:
                    act.wait_ge(stack_made, num(c) * HALVES + half - 1)
                cols = slice(half * C, (half + 1) * C)
                nc.scalar.activation(mid[:, cols], rest[:, cols], ACT.Copy, scale=part_sb[:, 1:2]) \
                    .then_inc(mid_made, 1)

            for t in range(CT):
                read_shift((None, 0), t)
                for part in range(2):
                    squares((None, 0), t, part)
            act.wait_ge(consts_set, 2)

            def step(c, first, last):
                nxt, prev = shifted(c, 1), shifted(c, -1)
                more = not late(last, 1)
                if not early(first, 1):
                    relu2(prev, 2)
                    relu2(prev, 3)
                read_moments(c)
                if more:
                    read_shift(nxt, 0)
                    squares(nxt, 0, 0)
                read_first_layer(c)
                for half in range(HALVES):
                    if not early(first, 1):
                        read_agg(prev, half)
                    relu1(c, half)
                if not early(first, 1):
                    middle_part(prev, 0)
                    middle_part(prev, 1)
                if more:
                    squares(nxt, 0, 1)
                    read_shift(nxt, 1)
                    squares(nxt, 1, 0)
                relu2(c, 0)
                relu2(c, 1)
                if more:
                    squares(nxt, 1, 1)

            steps(act, step)
            relu2((None, B - 1), 2)
            relu2((None, B - 1), 3)
            for half in range(HALVES):
                read_agg((None, B - 1), half)
                middle_part((None, B - 1), half)

        @block.gpsimd
        def _(pool):
            def per_block(v):
                return bass.AP(v.tensor, v.offset, [v.ap[0], v.ap[1], [0, POS]])

            def statistics(c):
                done = num(c) * STATS
                neg_mean, second = moments[:, 0, :], moments[:, 1, :]
                delta, delta2, var, rstd = (st[:, i, :] for i in range(4))
                pool.wait_ge(moments_read, num(c) * 2 + 1)
                nc.gpsimd.tensor_tensor(delta, neg_mean, shift64[:, slot(c), :], ALU.add) \
                    .then_inc(stat_steps, 1)
                pool.wait_ge(stat_steps, done + 1)
                nc.gpsimd.tensor_tensor(delta2, delta, delta, ALU.mult).then_inc(stat_steps, 1)
                pool.wait_ge(stat_steps, done + 2)
                pool.wait_ge(moments_read, num(c) * 2 + 2)
                nc.gpsimd.tensor_tensor(var, second, delta2, ALU.subtract).then_inc(stat_steps, 1)
                if c[0] is not None or c[1] > 0:
                    pool.wait_ge(ab_made, num(c))
                pool.wait_ge(pooled, num(c) * CT + CT)
                nc.gpsimd.tensor_tensor(norm[:], block_sum[:, slot(c)], per_block(neg_mean), ALU.add) \
                    .then_inc(stat_steps, 1)
                pool.wait_ge(stat_steps, done + 3)
                nc.gpsimd.tensor_tensor(rstd, var, half_pow[:], ALU.pow).then_inc(stat_steps, 1)
                pool.wait_ge(stat_steps, done + 5)
                nc.gpsimd.tensor_tensor(norm[:], norm[:], per_block(rstd), ALU.mult).then_inc(stat_steps, 1)

            def pair_sums(c):
                pool.wait_ge(first_read, num(c) + 1)
                if c[0] is not None or c[1] > 0:
                    pool.wait_ge(l2_made, num(c) * 4)
                for m in range(HT):
                    cen = centre[:, m, :]
                    cen3 = bass.AP(cen.tensor, cen.offset, [cen.ap[0], [0, 3], [GRID, GRID], [1, GRID]])
                    for ki in range(3):
                        row = neigh[:, m, ki * PADG:]
                        row3 = bass.AP(row.tensor, row.offset, [row.ap[0], [1, 3], [PADG, GRID], [1, GRID]])
                        dst = h1[:, m, ki * 3 * POS:(ki + 1) * 3 * POS] \
                            .rearrange("p (k i j) -> p k i j", k=3, i=GRID)
                        ins = nc.gpsimd.tensor_tensor(dst, row3, cen3, ALU.add)
                    ins.then_inc(pairs_made, 1)

            def fold(c, m):
                done = num(c) * FOLDS + m * FOLDS // HT
                pool.wait_ge(h2_ready, num(c) * 4 + 2 * m + 2)
                last = h2[:, m, 8 * POS:]
                for n, width in enumerate((4 * POS, 2 * POS, POS)):
                    if n:
                        pool.wait_ge(fold_steps, done + n)
                    nc.gpsimd.tensor_tensor(h2[:, m, 0:width], h2[:, m, 0:width], h2[:, m, width:2 * width],
                                            ALU.add).then_inc(fold_steps, 1)
                pool.wait_ge(fold_steps, done + 3)
                if m == 0 and (c[0] is not None or c[1] > 0):
                    pool.wait_ge(agg_made, num(c) * HALVES)

                def reached(ap):
                    return bass.AP(ap.tensor, ap.offset, [ap.ap[0], [POS - KPOS, HALVES], [0, PARTS], [1, KPOS]])

                nc.gpsimd.tensor_tensor(nb_sum[:, m], reached(h2[:, m, 0:POS]), reached(last),
                                        ALU.add).then_inc(fold_steps, 1)

            def rest_part(c, half):
                n = num(c) * HALVES + half
                pool.wait_ge(agg_read, n + 1)
                cols = slice(half * C, (half + 1) * C)
                if c[0] is not None or c[1] > 0:
                    pool.wait_ge(stack_made, num(c) * HALVES + half - 1)
                nc.gpsimd.tensor_tensor(rest[:, cols], agg[:, cols], high[:, cols], ALU.subtract) \
                    .then_inc(rest_made, 1)

            def stack_parts(c, half):
                n = num(c) * HALVES + half
                pool.wait_ge(mid_made, n + 1)
                cols = slice(half * C, (half + 1) * C)
                nc.gpsimd.tensor_tensor(stack[:, slot(c), cols], rest[:, cols], mid[:, cols], ALU.subtract) \
                    .then_inc(stack_made, 1)

            pool.wait_ge(consts_set, 2)

            def step(c, first, last):
                prev = shifted(c, -1)
                statistics(c)
                if not early(first, 1):
                    fold(prev, 1)
                pair_sums(c)
                if not early(first, 1):
                    for half in range(HALVES):
                        rest_part(prev, half)
                    for half in range(HALVES):
                        stack_parts(prev, half)
                fold(c, 0)

            steps(pool, step)
            fold((None, B - 1), 1)
            for half in range(HALVES):
                rest_part((None, B - 1), half)
                stack_parts((None, B - 1), half)


WEIGHT_DMAS = 6


def kernel(x, L0_conv_w1, L0_conv_b1, L0_conv_w2, L0_conv_b2, L0_conv_w3, L0_conv_b3):
    import numpy as np
    import concourse.bacc as bacc
    from concourse.bass_utils import run_bass_kernel_spmd

    B, C, H, W = x.shape
    taps = np.zeros((GRID, H), np.float32)
    for o in range(H):
        centre = (o + 0.5) * GRID / H - 0.5
        low = int(np.floor(centre))
        for j, weight in ((low, low + 1 - centre), (low + 1, centre - low)):
            taps[min(max(j, 0), GRID - 1), o] += weight
    up_w = np.zeros((PARTS, REACH * GRID, H, W), np.float32)
    for half, first in ((0, 0), (1, GRID - REACH)):
        rows = slice(half * H // 2, (half + 1) * H // 2)
        for i in range(REACH):
            for j in range(GRID):
                up_w[:, i * GRID + j, rows] = taps[first + i, rows, None] * taps[j, None, :]
    up_w = up_w.reshape(PARTS * REACH * GRID, H * W).astype("bfloat16")
    per_group = C // GROUPS
    same = np.kron(np.eye(P // per_group), np.ones((per_group, per_group)))
    group_w = np.stack([-64.0 * same, same]).astype(np.float32) / np.float32(per_group * H * W)
    part = np.repeat(np.arange(PARTS), REACH * GRID)
    part_w = np.stack([(part >= 1) / NB, part >= 2], axis=1).astype(np.float32)

    biases = np.concatenate([np.asarray(b).reshape(-1, P).T for b in (L0_conv_b1, L0_conv_b2, L0_conv_b3)], axis=1)

    ins = {"x": x, "w1": L0_conv_w1, "w2": L0_conv_w2, "w3": L0_conv_w3, "biases": biases, "up_w": up_w, "group_w": group_w, "part_w": part_w}
    nc = bacc.Bacc("TRN2", target_bir_lowering=False, num_devices=1)
    arrays = {f"{k}_dram": np.ascontiguousarray(v) for k, v in ins.items()}
    args = [nc.dram_tensor(k, v.shape, mybir.dt.from_np(v.dtype), kind="ExternalInput").ap()
            for k, v in arrays.items()]
    args.append(nc.dram_tensor("out_dram", (B, C, H, W), F32, kind="ExternalOutput").ap())
    conv_preact_program(nc, *args)
    return run_bass_kernel_spmd(nc, [arrays], core_ids=[0]).results[0]["out_dram"]
```
